# Optimizing a Trainium2 kernel written in Bass

```python
import numpy as np
import jax
import jax.numpy as jnp

def _softmax(x, axis=-1):
    return jax.nn.softmax(x, axis=axis)

def _gelu(x):
    return jax.nn.gelu(x, approximate=True)

def _silu(x):
    return jax.nn.silu(x)

def _sigmoid(x):
    return jax.nn.sigmoid(x)

def _layernorm(x, axis=-1, eps=1e-05):
    m = jnp.mean(x, axis=axis, keepdims=True)
    v = jnp.var(x, axis=axis, keepdims=True)
    return (x - m) / jnp.sqrt(v + eps)

def _scatter_add(tgt, idx, src, axis=0):
    return tgt.at[idx].add(src)

def _segment_sum(src, seg, n):
    return jax.ops.segment_sum(src, seg, n)
kernel_name = 'mk_gnn_preln_d2_gnn_r32_87a0b3'

def setup_inputs(seed: int=0):
    np.random.seed(seed)
    _w = jnp.asarray

    def _rec_inputs():
        import jax
        import jax.numpy as jnp
        _gk = jax.random.key(seed)
        x = -0.0003713 + 1 * jax.random.normal(jax.random.fold_in(_gk, 1), (3125, 128), jnp.float32)
        _s = jax.random.randint(jax.random.fold_in(_gk, 2), (25000,), 0, 3125, jnp.int32)
        _d = jax.random.randint(jax.random.fold_in(_gk, 3), (25000,), 0, 3125, jnp.int32)
        _loop = jnp.arange(3125, dtype=jnp.int32)
        src = jnp.concatenate([_s, _d, _loop])
        dst = jnp.concatenate([_d, _s, _loop])
        _o = jnp.argsort(dst, stable=True)
        src = src[_o]
        dst = dst[_o]
        return (x, src, dst)
    x, src, dst = _rec_inputs()

    def _L0_gnn_setup():
        import jax, jax.numpy as jnp
        import numpy as np
        N_NODES = 3125
        N_EDGES = 20000
        D_IN = 128
        D_OUT = 128
        key = jax.random.key(seed)
        k1, k2, k3, k4 = jax.random.split(key, 4)
        x = jax.random.normal(k1, (N_NODES, D_IN), dtype=jnp.float32)
        edge_index = jax.random.randint(k2, (2, N_EDGES), 0, N_NODES, dtype=jnp.int64)
        W = jax.random.normal(k3, (D_OUT, D_IN), dtype=jnp.float32) * 0.05
        b = jax.random.normal(k4, (D_OUT,), dtype=jnp.float32) * 0.05
        return {'x': x, 'edge_index': edge_index, 'W': W, 'b': b}
    _L0_gnn_all = _L0_gnn_setup()
    _L0_gnn_in = {k: v for k, v in _L0_gnn_all.items() if k in ('W', 'b')}
    del _L0_gnn_all

    def _L1_gnn_setup():
        import jax, jax.numpy as jnp
        import numpy as np
        N, E, D, T, L, DMLP = (3125, 25000, 128, 4, 2, 512)
        FIN = D // T
        AVG_LOG = float(np.log(17.0))
        LN_EPS = 1e-05

        def _layer_norm(x, g, b):
            mu = x.mean(-1, keepdims=True)
            var = jnp.var(x, axis=-1, keepdims=True)
            return (x - mu) / jnp.sqrt(var + LN_EPS) * g + b
        ks = jax.random.split(jax.random.key(seed), 10)
        s = 0.05
        return {'x': jax.random.normal(ks[0], (N, D), jnp.float32), 'edge_index': jax.random.randint(ks[1], (2, E), 0, N, jnp.int64) if jax.config.jax_enable_x64 else jax.random.randint(ks[1], (2, E), 0, N, jnp.int32), 'ln1_g': jnp.ones((L, D), jnp.float32), 'ln1_b': jnp.zeros((L, D), jnp.float32), 'W_pre': s * jax.random.normal(ks[2], (L, T, 2 * FIN, FIN), jnp.float32), 'b_pre': jnp.zeros((L, T, FIN), jnp.float32), 'W_post': s * jax.random.normal(ks[3], (L, T, 13 * FIN, FIN), jnp.float32), 'b_post': jnp.zeros((L, T, FIN), jnp.float32), 'W_lin': s * jax.random.normal(ks[4], (L, D, D), jnp.float32), 'b_lin': jnp.zeros((L, D), jnp.float32), 'ln2_g': jnp.ones((L, D), jnp.float32), 'ln2_b': jnp.zeros((L, D), jnp.float32), 'W1': s * jax.random.normal(ks[5], (L, D, DMLP), jnp.float32), 'b1': jnp.zeros((L, DMLP), jnp.float32), 'W2': s * jax.random.normal(ks[6], (L, DMLP, D), jnp.float32), 'b2': jnp.zeros((L, D), jnp.float32)}
    _L1_gnn_all = _L1_gnn_setup()
    _L1_gnn_in = {k: v for k, v in _L1_gnn_all.items() if k in ('ln1_g', 'ln1_b', 'W_pre', 'b_pre', 'W_post', 'b_post', 'W_lin', 'b_lin', 'ln2_g', 'ln2_b', 'W1', 'b1', 'W2', 'b2')}
    del _L1_gnn_all
    return {'x': x, 'src': src, 'dst': dst, 'L0_gnn_W': _L0_gnn_in['W'], 'L0_gnn_b': _L0_gnn_in['b'], 'L1_gnn_ln1_g': _L1_gnn_in['ln1_g'], 'L1_gnn_ln1_b': _L1_gnn_in['ln1_b'], 'L1_gnn_W_pre': _L1_gnn_in['W_pre'], 'L1_gnn_b_pre': _L1_gnn_in['b_pre'], 'L1_gnn_W_post': _L1_gnn_in['W_post'], 'L1_gnn_b_post': _L1_gnn_in['b_post'], 'L1_gnn_W_lin': _L1_gnn_in['W_lin'], 'L1_gnn_b_lin': _L1_gnn_in['b_lin'], 'L1_gnn_ln2_g': _L1_gnn_in['ln2_g'], 'L1_gnn_ln2_b': _L1_gnn_in['ln2_b'], 'L1_gnn_W1': _L1_gnn_in['W1'], 'L1_gnn_b1': _L1_gnn_in['b1'], 'L1_gnn_W2': _L1_gnn_in['W2'], 'L1_gnn_b2': _L1_gnn_in['b2']}

def reference(x, src, dst, L0_gnn_W, L0_gnn_b, L1_gnn_ln1_g, L1_gnn_ln1_b, L1_gnn_W_pre, L1_gnn_b_pre, L1_gnn_W_post, L1_gnn_b_post, L1_gnn_W_lin, L1_gnn_b_lin, L1_gnn_ln2_g, L1_gnn_ln2_b, L1_gnn_W1, L1_gnn_b1, L1_gnn_W2, L1_gnn_b2):
    import jax
    import jax.numpy as jnp

    def _L0_gnn_ref(x, edge_index, W, b):
        import jax, jax.numpy as jnp
        import numpy as np
        N_NODES = 3125
        N_EDGES = 20000
        D_IN = 128
        D_OUT = 128
        src, dst = (edge_index[0], edge_index[1])
        n = x.shape[0]
        ones = jnp.ones(src.shape[0], dtype=x.dtype)
        deg = jax.ops.segment_sum(ones, src, num_segments=n) + jax.ops.segment_sum(ones, dst, num_segments=n)
        deg_inv_sqrt = jnp.where(deg > 0, jax.lax.rsqrt(deg), 0.0)
        norm = deg_inv_sqrt[src] * deg_inv_sqrt[dst]
        msg_to_dst = norm[:, None] * x[src]
        msg_to_src = norm[:, None] * x[dst]
        out = x + jax.ops.segment_sum(msg_to_dst, dst, num_segments=n) + jax.ops.segment_sum(msg_to_src, src, num_segments=n)
        return jax.nn.relu(out @ W.T + b)

    def _L1_gnn_ref(x, edge_index, ln1_g, ln1_b, W_pre, b_pre, W_post, b_post, W_lin, b_lin, ln2_g, ln2_b, W1, b1, W2, b2):
        import jax, jax.numpy as jnp
        import numpy as np
        N, E, D, T, L, DMLP = (3125, 25000, 128, 4, 2, 512)
        FIN = D // T
        AVG_LOG = float(np.log(17.0))
        LN_EPS = 1e-05

        def _layer_norm(x, g, b):
            mu = x.mean(-1, keepdims=True)
            var = jnp.var(x, axis=-1, keepdims=True)
            return (x - mu) / jnp.sqrt(var + LN_EPS) * g + b
        n, d = x.shape
        src, dst = (edge_index[0], edge_index[1])
        cnt = jax.ops.segment_sum(jnp.ones(src.shape, x.dtype), dst, num_segments=n)
        deg = jnp.maximum(cnt, 1.0)
        amp = (jnp.log(deg + 1.0) / AVG_LOG)[:, None, None]
        att = (AVG_LOG / jnp.log(deg + 1.0))[:, None, None]
        has = (cnt > 0)[:, None, None]
        denom = deg[:, None, None]
        for l in range(ln1_g.shape[0]):
            h = _layer_norm(x, ln1_g[l], ln1_b[l]).reshape(n, T, FIN)
            m = jnp.concatenate([h[dst], h[src]], axis=-1)
            m = jnp.einsum('etf,tfg->etg', m, W_pre[l]) + b_pre[l]
            mean = jax.ops.segment_sum(m, dst, num_segments=n) / denom
            mean2 = jax.ops.segment_sum(m * m, dst, num_segments=n) / denom
            std = jnp.sqrt(jax.nn.relu(mean2 - mean * mean) + 1e-05)
            mn = jnp.where(has, jax.ops.segment_min(m, dst, num_segments=n), 0.0)
            mx = jnp.where(has, jax.ops.segment_max(m, dst, num_segments=n), 0.0)
            aggs = jnp.concatenate([mean, mn, mx, std], axis=-1)
            agg = jnp.concatenate([aggs, aggs * amp, aggs * att], -1)
            comb = jnp.concatenate([h, agg], axis=-1)
            o = jnp.einsum('ntf,tfg->ntg', comb, W_post[l]) + b_post[l]
            o = o.reshape(n, d) @ W_lin[l] + b_lin[l]
            x = x + o
            h2 = _layer_norm(x, ln2_g[l], ln2_b[l])
            h2 = jax.nn.gelu(h2 @ W1[l] + b1[l], approximate=False) @ W2[l] + b2[l]
            x = x + h2
        return x
    edge_index = jnp.stack([src, dst])
    h = jnp.maximum(_layernorm(x, axis=-1), 0.0)
    x = x + _L0_gnn_ref(h, edge_index, L0_gnn_W, L0_gnn_b)
    h = jnp.maximum(_layernorm(x, axis=-1), 0.0)
    x = x + _L1_gnn_ref(h, edge_index, L1_gnn_ln1_g, L1_gnn_ln1_b, L1_gnn_W_pre, L1_gnn_b_pre, L1_gnn_W_post, L1_gnn_b_post, L1_gnn_W_lin, L1_gnn_b_lin, L1_gnn_ln2_g, L1_gnn_ln2_b, L1_gnn_W1, L1_gnn_b1, L1_gnn_W2, L1_gnn_b2)
    return x

_drawn_inputs = setup_inputs


def setup_inputs(seed=0):
    import zlib

    import numpy as np

    out = dict(_drawn_inputs(seed))
    spreads = {'L1_gnn_ln1_g': (1.0, 0.2),
     'L1_gnn_ln1_b': (0.0, 0.347),
     'L1_gnn_b_pre': (0.0, 0.1),
     'L1_gnn_b_post': (0.0, 0.1),
     'L1_gnn_b_lin': (0.0, 0.1),
     'L1_gnn_ln2_g': (1.0, 0.2),
     'L1_gnn_ln2_b': (0.0, 0.1),
     'L1_gnn_b1': (0.0, 0.1),
     'L1_gnn_b2': (0.0, 0.1)}
    factors = {}
    for name, (base, spread) in spreads.items():
        noise = np.random.default_rng([zlib.crc32(name.encode()), seed]).standard_normal(out[name].shape)
        drawn = base * np.exp(spread * noise) if base else spread * noise
        out[name] = jnp.asarray(drawn.astype(out[name].dtype))
    for name, factor in factors.items():
        out[name] = (out[name] * factor).astype(out[name].dtype)
    return out
```

```python
from contextlib import ExitStack

import numpy as np

import concourse.bass as bass
from concourse import mybir

F32 = mybir.dt.float32
BF16 = mybir.dt.bfloat16
I32 = mybir.dt.int32
ALU = mybir.AluOpType
ACT = mybir.ActivationFunctionType

P = 128
N, E, D, DM, TOWERS, LAYERS = 3125, 53125, 128, 512, 4, 2
FIN = D // TOWERS
CHUNKS = 13
NB = -(-N // P)
K = -(-E // P)
G = 4
R = 4
ITERS = K // (G * R)
GROUPS = K // G
U = 5
SPREAD = 32
HC = 16
BIG = 1.7e38
EPS = 1e-5
AVG_LOG = float(np.log(17.0))
PHASES = 1 + LAYERS
assert K == ITERS * G * R and NB % U == 0 and K % HC == 0


def over_blocks(eng, stages):
    for t in range(U):
        for stage, lag in stages:
            if t >= lag:
                stage(t - lag, t - lag, 0)
    with eng.Fori(1, NB // U) as i:
        for t in range(U):
            for stage, lag in stages:
                stage(i * U + (t - lag), (t - lag) % U, i + (t - lag) // U)
    for t in range(NB, NB + max(lag for _, lag in stages)):
        for stage, lag in stages:
            if t - lag < NB:
                stage(t - lag, (t - lag) % U, (t - lag) // U)


def pair_free(n, j):
    if isinstance(n, int):
        return max(0, n if j == 0 else n - 1)
    return n if j == 0 else n - 1


def ring_free(n):
    return max(0, n - (U - 1)) if isinstance(n, int) else n - (U - 1)


def graph_layers(nc, x, src, dst, W, b, ln1_g, ln1_b, W_pre, b_pre, W_post, b_post, W_lin, b_lin,
                 ln2_g, ln2_b, W1, b1, W2, b2, out):
    with ExitStack() as ctx:
        def sb(name, shape, dt=F32):
            return ctx.enter_context(nc.sbuf_tensor(name, shape, dt))

        def sem(name):
            return ctx.enter_context(nc.semaphore(name))

        table = [nc.dram_tensor(f"table{q}", (NB * P, D), F32).ap() for q in range(PHASES)]
        states = [nc.dram_tensor(f"states{q}", (P * K, D if q == 0 else 4 * D), F32).ap()
                  for q in range(PHASES)]

        xin = sb("xin", [P, NB * D])
        cur = sb("cur", [P, NB * D])
        acc = sb("acc", [P, NB * D])
        own = sb("own", [P, NB * D])
        bn = sb("bn", [P, NB * 6])
        mean = sb("mean", [P, NB])
        gap = sb("gap", [P, NB])
        vsum = sb("vsum", [P, NB])
        rowvar = sb("rowvar", [P, NB])
        rstd = sb("rstd", [P, NB])
        nmr = sb("nmr", [P, NB])
        std_t = sb("std_t", [P, NB])
        cnt = sb("cnt", [P, NB])
        tot = sb("tot", [P, NB])
        totscan = sb("totscan", [P, NB])
        end_f = sb("end_f", [P, NB])
        end_i = sb("end_i", [P, NB], I32)
        has = sb("has", [P, NB])
        nhas = sb("nhas", [P, NB])
        deg = sb("deg", [P, NB])
        inv = sb("inv", [P, NB])
        dis = sb("dis", [P, NB])
        dis2 = sb("dis2", [P, NB])
        amp = sb("amp", [P, NB])
        att = sb("att", [P, NB])
        tmpn = sb("tmpn", [P, 5, NB])
        src_i = sb("src_i", [P, K + R * G], I32)
        dst_i = sb("dst_i", [P, K], I32)
        part_i = sb("part_i", [P, 2, K], I32)
        part_f = sb("part_f", [P, 2, K])
        dst_f = sb("dst_f", [P, K])
        prev_i = sb("prev_i", [P, 1], I32)
        prev_f = sb("prev_f", [P, 1])
        keep = sb("keep", [P, K])
        lim = sb("lim", [P, K])
        runlen = sb("runlen", [P, 1])
        fix_i = sb("fix_i", [P, 1], I32)
        base_i = sb("base_i", [P, 1], I32)
        base_f = sb("base_f", [P, 1])
        carry_in = sb("carry_in", [P, 1])
        carry_lim = sb("carry_lim", [P, 1])
        pass_on = sb("pass_on", [P, 1])
        pass_row = sb("pass_row", [P, P])
        pass_lim = sb("pass_lim", [P, P])
        iota_i = sb("iota_i", [P, P], I32)
        iota_f = sb("iota_f", [P, P])
        iota_b = sb("iota_b", [P, P], BF16)
        lane_i = sb("lane_i", [P, 1], I32)
        lane_f = sb("lane_f", [P, 1])
        ident = sb("ident", [P, P])
        ones = sb("ones", [P, P])
        tri = sb("tri", [P, P])
        zero_b = sb("zero_b", [P, P], BF16)
        diag = sb("diag", [P, P])
        epsc = sb("epsc", [P, 1])
        idx = sb("idx", [P, R, G], I32)
        rows = sb("rows", [P, R, G, 3 * D])
        state = sb("state", [P, R, G, 4 * D])
        carry = sb("carry", [P, 4, P + 1])
        fixrow = sb("fixrow", [P, 4 * D])
        fixed = sb("fixed", [P, 4 * D])
        msq = sb("msq", [P, U, D])
        var = sb("var", [P, U, D])
        turned = sb("turned", [P, U, 4 * D])
        znorm = sb("znorm", [P, U, D])
        bout = sb("bout", [P, U, D])
        part1 = sb("part1", [P, U, D])
        part2 = sb("part2", [P, U, D])
        slots = state[:].rearrange("p r g f -> p (r g) f")
        agg = slots[:, 0:U]
        hid = slots[:, U:2 * U]
        nst = rows[:].rearrange("p r g f -> p (r g f)")[:, 0:U * 4 * D].rearrange(
            "p (j f) -> p j f", j=U)
        lo_words, hi_words = HC * P, HC * SPREAD
        codes = state[:].rearrange("p r g f -> p (r g f)")[:, 0:lo_words + hi_words].bitcast(BF16)
        onehot_lo = codes[:, 0:2 * lo_words].rearrange("p (h k c) -> p h k c", h=2, k=HC)
        onehot_hi = codes[:, 2 * lo_words:2 * (lo_words + hi_words)].rearrange(
            "p (h k c) -> p h k c", h=2, k=HC)
        w0 = sb("w0", [P, D])
        w0t = sb("w0t", [P, D])
        b0row = sb("b0row", [P, D])
        g1c = sb("g1c", [P, LAYERS])
        c1c = sb("c1c", [P, LAYERS])
        g2c = sb("g2c", [P, LAYERS])
        c2c = sb("c2c", [P, LAYERS])
        b1c = sb("b1c", [P, LAYERS, DM // P])
        bpostc = sb("bpostc", [P, LAYERS])
        bprerow = sb("bprerow", [P, LAYERS, D])
        blinrow = sb("blinrow", [P, LAYERS, D])
        b2row = sb("b2row", [P, LAYERS, D])
        wlin = sb("wlin", [P, LAYERS, D])
        w1 = sb("w1", [P, LAYERS, DM])
        w2 = sb("w2", [P, LAYERS, DM // P, D])
        post = sb("post", [P, LAYERS, CHUNKS, D])
        post_t = sb("post_t", [P, 4, D])
        postbc = sb("postbc", [P, LAYERS, P])
        hrow = sb("hrow", [P, LAYERS, D])
        wcat = sb("wcat", [P, LAYERS, 3 * D])
        wagg = sb("wagg", [P, LAYERS, 4, 3 * D])

        ps_t = [ctx.enter_context(nc.psum_tensor(f"ps_t{i}", [P, 512], F32)) for i in range(2)]
        ps_m = [ctx.enter_context(nc.psum_tensor(f"ps_m{i}", [P, 512], F32)) for i in range(2)]
        ps_o = [ctx.enter_context(nc.psum_tensor(f"ps_o{i}", [P, 512], F32)) for i in range(2)]
        ps_c = ctx.enter_context(nc.psum_tensor("ps_c", [P, 512], F32))
        ps_s = ctx.enter_context(nc.psum_tensor("ps_s", [P, 512], F32))

        blank = sem("blank")
        edges_in = sem("edges_in")
        x_in = sem("x_in")
        small_in = sem("small_in")
        weights_in = sem("weights_in")
        post_in = sem("post_in")
        iotas = sem("iotas")
        consts = sem("consts")
        prep = sem("prep")
        coded = sem("coded")
        counted = sem("counted")
        cnt_ready = sem("cnt_ready")
        prefix_t = sem("prefix_t")
        dis_in = sem("dis_in")
        dis_root = sem("dis_root")
        dis_ready = sem("dis_ready")
        log_in = sem("log_in")
        logs = sem("logs")
        bn_v = sem("bn_v")
        moment_v = sem("moment_v")
        root_a = sem("root_a")
        norm_v = sem("norm_v")
        nrm_v = sem("nrm_v")
        relu_a = sem("relu_a")
        y_a = sem("y_a")
        table_in = sem("table_in")
        idx_ready = [sem(f"idx_ready{g}") for g in range(R)]
        begun = sem("begun")
        gathered = [sem(f"gathered{g}") for g in range(R)]
        lifted = sem("lifted")
        scanned = sem("scanned")
        stored = [sem(f"stored{g}") for g in range(R)]
        ends_t = sem("ends_t")
        carried = sem("carried")
        carry_t = sem("carry_t")
        fix_in = sem("fix_in")
        fix_v = sem("fix_v")
        fix_out = sem("fix_out")
        fold_t = sem("fold_t")
        fold_tc = sem("fold_tc")
        fold_m = sem("fold_m")
        fold_mc = sem("fold_mc")
        post_bc = sem("post_bc")
        post_row = sem("post_row")
        hrow_v = sem("hrow_v")
        nst_in = [sem(f"nst_in{j}") for j in range(U)]
        sq_a = sem("sq_a")
        var_v = sem("var_v")
        agg_v = sem("agg_v")
        std_a = sem("std_a")
        z_v = sem("z_v")
        turned_pe = sem("turned_pe")
        turned_a = sem("turned_a")
        mm_pe = sem("mm_pe")
        hid_a = sem("hid_a")
        out_pe = sem("out_pe")
        own_a = sem("own_a")
        bout_v = sem("bout_v")
        bout_st = [sem(f"bout_st{j}") for j in range(U)]
        xa_v = sem("xa_v")
        xb_v = sem("xb_v")
        x_v = sem("x_v")
        acc_v = sem("acc_v")
        out_v = sem("out_v")
        out_st = sem("out_st")

        def blk(t, n):
            return t[:, n * D:(n + 1) * D] if isinstance(n, int) else t[:, bass.ds(n * D, D)]

        def col(t, n):
            return t[:, n:n + 1] if isinstance(n, int) else t[:, bass.ds(n, 1)]

        def node_rows(t):
            return t.rearrange("(b p) f -> p b f", p=P)

        bn3 = bn[:].rearrange("p (b c) -> p b c", c=6)

        def first_pass(kind, l=0):
            return {"first": 0, "table": 1, "stats": 2, "mlp": 3}[kind] + 3 * l

        def norm_pass(kind, l=0):
            return {"lead": 0, "first": 1, "relu": 2, "stats": 3, "mlp": 4}[kind] + 2 * l

        def x_pass(kind, l=0):
            return {"first": 0, "stats": 1, "mlp": 2}[kind] + 2 * l

        def per_step(q):
            return 1 if q == 0 else 2

        def scanned_before(q):
            return K * (0 if q == 0 else 2 * q - 1)

        n_small = 16 * (1 + LAYERS * (4 + 1 + DM // P + 3))
        n_weights = 16 * (3 + LAYERS + 2 * LAYERS * TOWERS)

        block = ctx.enter_context(nc.Block())

        @block.sync
        def _(sp):
            sp.wait_ge(blank, 1)
            sp.dma_start(dst_i[:], dst.rearrange("(p k) -> p k", p=P)).then_inc(edges_in, 16)
            sp.dma_start(prev_i[1:P, :], dst.rearrange("(p k) -> p k", p=P)[0:P - 1, K - 1:K],
                         allow_slow_non_contiguous=True).then_inc(edges_in, 16)
            sp.dma_start(xin[:].rearrange("p (b f) -> p b f", f=D), node_rows(x)).then_inc(x_in, 16)
            sp.dma_start(src_i[:, 0:K], src.rearrange("(p k) -> p k", p=P)).then_inc(edges_in, 16)
            sp.dma_start(src_i[:, K:K + R * G], src.rearrange("(p k) -> p k", p=P)[:, 0:R * G]
                         ).then_inc(edges_in, 16)
            sp.dma_start(w0[:], W).then_inc(weights_in, 16)
            sp.dma_start(wlin[:], W_lin.rearrange("l g o -> g l o")).then_inc(weights_in, 16)
            sp.wait_ge(blank, 2)
            for l in range(LAYERS):
                for t in range(TOWERS):
                    r = slice(t * FIN, (t + 1) * FIN)
                    sp.dma_start(wcat[r, l, t * FIN:(t + 1) * FIN],
                                 W_pre[l, t, FIN:2 * FIN, :]).then_inc(weights_in, 16)
                    sp.dma_start(wcat[r, l, 2 * D + t * FIN:2 * D + (t + 1) * FIN],
                                 W_pre[l, t, 0:FIN, :]).then_inc(weights_in, 16)
                    sp.dma_start(post[r, l, :, t * FIN:(t + 1) * FIN],
                                 W_post[l, t].rearrange("(c f) g -> f c g", f=FIN)
                                 ).then_inc(post_in, 16)
            sp.dma_start(w1[:], W1.rearrange("l f m -> f l m")).then_inc(weights_in, 16)
            for l in range(LAYERS):
                sp.dma_start(w2[:, l], W2[l].rearrange("(j m) f -> m j f", m=P)
                             ).then_inc(weights_in, 16)

            for q in range(PHASES):
                if q == 0:
                    sp.wait_ge(y_a, NB)
                    sp.dma_start(node_rows(table[0]), own[:].rearrange("p (b f) -> p b f", f=D)
                                 ).then_inc(table_in, 16)
                else:
                    def store_table(n, j, turn):
                        sp.wait_ge(bout_v, n + ((q - 1) * NB + 1))
                        at = (table[q][n * P:(n + 1) * P, :] if isinstance(n, int)
                              else table[q][bass.ds(n * P, P), :])
                        sp.dma_start(at, bout[:, j]).then_inc(bout_st[j], 16)
                    over_blocks(sp, [(store_table, 0)])
                view = states[q].rearrange("(p k) f -> p k f", k=K)
                inc = G * per_step(q)
                with sp.Fori(0, ITERS) as i:
                    for g in range(R):
                        sp.wait_ge(scanned, i * (R * inc) + (scanned_before(q) + (g + 1) * inc))
                        piece = state[:, g, :, 2 * D:3 * D] if q == 0 else state[:, g]
                        sp.dma_start(view[:, bass.ds(i * (R * G) + g * G, G), :], piece
                                     ).then_inc(stored[g], 16)
            sp.wait_ge(out_v, NB)
            sp.dma_start(node_rows(out), acc[:].rearrange("p (b f) -> p b f", f=D)
                         ).then_inc(out_st, 16)
            sp.wait_ge(out_st, 16)

        @block.gpsimd
        def _(pool):
            pool.iota(iota_i[:], pattern=[[1, P]], base=0, channel_multiplier=0)
            pool.iota(lane_i[:], pattern=[[0, 1]], base=0, channel_multiplier=1)
            pool.iota(base_i[:], pattern=[[0, 1]], base=0, channel_multiplier=K
                      ).then_inc(iotas, 1)
            for q in range(PHASES):
                if q == 0:
                    pool.wait_ge(table_in, 16)
                else:
                    for j in range(U):
                        pool.wait_ge(bout_st[j], 16 * (NB // U) * q)
                with pool.Fori(0, ITERS) as i:
                    for g in range(R):
                        pool.wait_ge(idx_ready[g], i + (q * ITERS + 1))
                        pool.sem_inc(begun, 1)
                        for j in range(G):
                            pool.indirect_dma_start(
                                rows[:, g, j, D:2 * D], None, table[q],
                                bass.IndirectOffsetOnAxis(ap=idx[:, g, j:j + 1], axis=0)
                            ).then_inc(gathered[g], 16)
                w = D if q == 0 else 4 * D
                for g in range(R):
                    pool.wait_ge(stored[g], 16 * ITERS * (q + 1))
                pool.indirect_dma_start(
                    fixrow[:, 0:w], None, states[q],
                    bass.IndirectOffsetOnAxis(ap=fix_i[:, 0:1], axis=0)).then_inc(fix_in, 16)
                pool.wait_ge(fix_v, 2 * q + 1)
                pool.indirect_dma_start(
                    states[q], bass.IndirectOffsetOnAxis(ap=fix_i[:, 0:1], axis=0),
                    fixed[:, 0:w], None).then_inc(fix_out, 16)
                pool.wait_ge(fix_out, 16 * (q + 1))
                for n in range(NB):
                    if n >= U:
                        pool.wait_ge(agg_v, q * NB + n - U + 1)
                    pool.indirect_dma_start(
                        nst[:, n % U, 0:w], None, states[q],
                        bass.IndirectOffsetOnAxis(ap=end_i[:, n:n + 1], axis=0)
                    ).then_inc(nst_in[n % U], 16)

        @block.scalar
        def _(act):
            def over_partitions(v):
                return v.rearrange("(o f) -> o f", o=1).to_broadcast([P, v.shape[0]])

            def column(v):
                return v.rearrange("(f o) -> f o", o=1)

            slow = dict(allow_slow_non_contiguous=True)
            act.dma_start(b0row[:], over_partitions(b)).then_inc(small_in, 16)
            for l in range(LAYERS):
                for dst_t, v in ((g1c, ln1_g), (c1c, ln1_b), (g2c, ln2_g), (c2c, ln2_b)):
                    act.dma_start(dst_t[:, l:l + 1], column(v[l]), **slow).then_inc(small_in, 16)
                act.dma_start(bpostc[:, l:l + 1], column(b_post[l].rearrange("t g -> (t g)")),
                              **slow).then_inc(small_in, 16)
                for j in range(DM // P):
                    act.dma_start(b1c[:, l, j:j + 1], column(b1[l, j * P:(j + 1) * P]),
                                  **slow).then_inc(small_in, 16)
                act.dma_start(bprerow[:, l], over_partitions(b_pre[l].rearrange("t g -> (t g)"))
                              ).then_inc(small_in, 16)
                act.dma_start(blinrow[:, l], over_partitions(b_lin[l])).then_inc(small_in, 16)
                act.dma_start(b2row[:, l], over_partitions(b2[l])).then_inc(small_in, 16)

            def roots(t):
                act.wait_ge(moment_v, 3 * (t + 1))
                nc.scalar.activation(std_t[:], rowvar[:], ACT.Sqrt, bias=epsc[:, 0:1]
                                     ).then_inc(root_a, 1)

            act.wait_ge(consts, 1)
            roots(norm_pass("lead"))
            act.wait_ge(norm_v, norm_pass("lead") + 1)

            def relu_of_norm(dst_t):
                def stage(n, j, turn):
                    nc.scalar.activation(blk(dst_t, n), blk(xin, n), ACT.Relu, bias=col(nmr, n),
                                         scale=col(rstd, n)).then_inc(relu_a, 1)
                return stage

            over_blocks(act, [(relu_of_norm(acc), 0)])
            act.wait_ge(dis_in, 1)
            nc.scalar.activation(tmpn[:, 0], dis[:], ACT.Sqrt).then_inc(dis_root, 1)
            act.wait_ge(dis_ready, 1)
            act.wait_ge(relu_a, NB)

            def scale_y(n, j, turn):
                nc.scalar.activation(blk(own, n), blk(acc, n), ACT.Identity, scale=col(dis, n)
                                     ).then_inc(y_a, 1)

            over_blocks(act, [(scale_y, 0)])
            act.wait_ge(log_in, 1)
            nc.scalar.activation(tmpn[:, 1], amp[:], ACT.Ln).then_inc(logs, 1)

            act.wait_ge(fold_t, 1)
            nc.scalar.copy(w0t[:], ps_o[0][:, 0:D]).then_inc(fold_tc, 1)
            act.wait_ge(blank, 2)
            for l in range(LAYERS):
                for c0 in range(0, CHUNKS, 4):
                    m = min(4, CHUNKS - c0)
                    step = l * 4 + c0 // 4
                    act.wait_ge(fold_t, step + 2)
                    act.wait_ge(fold_m, step)
                    nc.scalar.copy(post_t[:, 0:m], ps_o[0][:, 0:m * D].rearrange(
                        "p (c f) -> p c f", f=D)).then_inc(fold_tc, 1)
                    act.wait_ge(fold_m, step + 1)
                    for c in range(c0, c0 + m):
                        to = (wcat[:, l, D:2 * D] if c == 0 else
                              wagg[:, l, (c - 1) % 4, (c - 1) // 4 * D:((c - 1) // 4 + 1) * D])
                        last = nc.scalar.copy(to, ps_o[1][:, (c - c0) * D:(c - c0 + 1) * D])
                    last.then_inc(fold_mc, 1)

            t0 = first_pass("first") * NB

            def copy_turned(t, w, freed=mm_pe, scale=None, bias=None):
                def stage(n, j, turn):
                    act.wait_ge(turned_pe, n + (t + 1))
                    act.wait_ge(freed, ring_free(n) + t)
                    if scale is None:
                        nc.scalar.copy(turned[:, j, 0:w], ps_t[j % 2][:, 0:w]
                                       ).then_inc(turned_a, 1)
                    else:
                        nc.scalar.activation(turned[:, j, 0:w], ps_t[j % 2][:, 0:w], ACT.Identity,
                                             bias=bias, scale=scale).then_inc(turned_a, 1)
                return stage

            over_blocks(act, [(copy_turned(t0, D), 0)])
            roots(norm_pass("first"))
            act.wait_ge(norm_v, norm_pass("first") + 1)
            over_blocks(act, [(relu_of_norm(cur), 0)])
            roots(norm_pass("relu"))

            act.wait_ge(small_in, n_small)
            for l in range(LAYERS):
                t0 = first_pass("table", l) * NB

                def keep_own(n, j, turn):
                    act.wait_ge(mm_pe, n + (t0 + 1))
                    nc.scalar.activation(blk(own, n), ps_o[j % 2][:, 0:D], ACT.Identity,
                                         scale=col(has, n)).then_inc(own_a, 1)

                over_blocks(act, [(copy_turned(t0, D, scale=g1c[:, l:l + 1], bias=c1c[:, l:l + 1]), 0),
                                  (keep_own, 1)])

                with act.Fori(0, ITERS) as i:
                    for g in range(R):
                        act.wait_ge(gathered[g], i * (16 * G) + 16 * G * (ITERS * (l + 1) + 1))
                        b_rows = rows[:, g, :, D:2 * D]
                        nc.scalar.mul(rows[:, g, :, 0:D], b_rows, -1.0)
                        nc.scalar.square(rows[:, g, :, 2 * D:3 * D], b_rows).then_inc(lifted, 1)

                t0 = first_pass("stats", l) * NB

                def square_mean(n, j, turn):
                    act.wait_ge(nst_in[j], turn * 16 + 16 * (NB // U * (l + 1) + 1))
                    nc.scalar.activation(msq[:, j], nst[:, j, 2 * D:3 * D], ACT.Square,
                                         scale=col(inv, n)).then_inc(sq_a, 1)

                def root_var(n, j, turn):
                    act.wait_ge(agg_v, n + ((l + 1) * NB + 1))
                    nc.scalar.activation(agg[:, j, 3 * D:4 * D], var[:, j], ACT.Sqrt,
                                         bias=epsc[:, 0:1]).then_inc(std_a, 1)

                over_blocks(act, [(square_mean, 0), (root_var, 1), (copy_turned(t0, 4 * D), 2)])
                roots(norm_pass("stats", l))

                t0 = first_pass("mlp", l) * NB

                def gelu(n, j, turn):
                    act.wait_ge(mm_pe, n + (t0 + 1))
                    act.wait_ge(out_pe, ring_free(n) + l * NB)
                    for c in range(DM // P):
                        last = nc.scalar.activation(
                            hid[:, j, c * P:(c + 1) * P], ps_m[j % 2][:, c * P:(c + 1) * P],
                            ACT.Gelu, bias=b1c[:, l, c:c + 1])
                    last.then_inc(hid_a, 1)

                over_blocks(act, [(copy_turned(t0, D, scale=g2c[:, l:l + 1], bias=c2c[:, l:l + 1]), 0),
                                  (gelu, 1)])
                if l < LAYERS - 1:
                    roots(norm_pass("mlp", l))

        @block.tensor
        def _(pe):
            pe.wait_ge(consts, 1)
            nc.tensor.matmul(ps_c[:, 0:SPREAD], zero_b[:], zero_b[:, 0:SPREAD],
                             start=True, stop=False, skip_group_check=True)
            with pe.Fori(0, K // HC // 2) as i:
                for h in range(2):
                    pe.wait_ge(coded, i * 2 + (h + 1))
                    for k in range(HC):
                        last = nc.tensor.matmul(ps_c[:, 0:SPREAD], onehot_lo[:, h, k],
                                                onehot_hi[:, h, k], start=False, stop=False,
                                                skip_group_check=True)
                    last.then_inc(counted, 1)
            nc.tensor.matmul(ps_c[:, 0:SPREAD], zero_b[:], zero_b[:, 0:SPREAD],
                             start=False, stop=True, skip_group_check=True).then_inc(counted, 1)
            pe.wait_ge(cnt_ready, 1)
            nc.tensor.matmul(ps_s[:, 0:NB], tri[:], cnt[:], start=True, stop=True)
            nc.tensor.matmul(ps_s[:, SPREAD:SPREAD + NB], ones[:], cnt[:], start=True, stop=True)
            nc.tensor.matmul(ps_s[:, P:2 * P], ones[:], diag[:], start=True, stop=True
                             ).then_inc(prefix_t, 1)

            pe.wait_ge(weights_in, n_weights)
            pe.wait_ge(post_in, 16 * LAYERS * TOWERS)
            nc.tensor.transpose(ps_o[0][:, 0:D], w0[:], ident[:]).then_inc(fold_t, 1)
            for l in range(LAYERS):
                for c0 in range(0, CHUNKS, 4):
                    m = min(4, CHUNKS - c0)
                    step = l * 4 + c0 // 4
                    pe.wait_ge(fold_tc, step + 1)
                    for c in range(m):
                        last = nc.tensor.transpose(ps_o[0][:, c * D:(c + 1) * D],
                                                   post[:, l, c0 + c], ident[:])
                    last.then_inc(fold_t, 1)
                    pe.wait_ge(fold_tc, step + 2)
                    pe.wait_ge(fold_mc, step)
                    for c in range(m):
                        last = nc.tensor.matmul(ps_o[1][:, c * D:(c + 1) * D], post_t[:, c],
                                                wlin[:, l], start=True, stop=True)
                    last.then_inc(fold_m, 1)
                pe.wait_ge(post_bc, l + 1)
                nc.tensor.matmul(ps_m[0][:, l * D:(l + 1) * D], postbc[:, l], wlin[:, l], start=True, stop=True
                                 ).then_inc(post_row, 1)

            def ends(q):
                s = [2] if q == 0 else list(range(4))
                pe.wait_ge(scanned, scanned_before(q + 1))
                for a, c in enumerate(s):
                    last = nc.tensor.transpose(ps_c[:, a * P:(a + 1) * P],
                                               state[:, R - 1, G - 1, c * D:(c + 1) * D], ident[:])
                last.then_inc(ends_t, 1)
                pe.wait_ge(carried, q + 1)
                for a, c in enumerate(s):
                    last = nc.tensor.transpose(ps_s[:, a * P:(a + 1) * P], carry[:, a, 0:P],
                                               ident[:])
                last.then_inc(carry_t, 1)

            def turn(t, source, w, ready, ready_base):
                def stage(n, j, turn_):
                    pe.wait_ge(ready, n + (ready_base + 1))
                    pe.wait_ge(turned_a, pair_free(n, j) + t)
                    for c in range(w // D):
                        last = nc.tensor.transpose(ps_t[j % 2][:, c * D:(c + 1) * D],
                                                   source[:, j, c * D:(c + 1) * D], ident[:])
                    last.then_inc(turned_pe, 1)
                return stage

            ends(0)
            t0 = first_pass("first") * NB
            pe.wait_ge(hrow_v, LAYERS)

            def times_w(n, j, turn_):
                pe.wait_ge(turned_a, n + (t0 + 1))
                pe.wait_ge(xa_v, pair_free(n, j) + t0)
                nc.tensor.matmul(ps_m[j % 2][:, 0:D], turned[:, j, 0:D], w0t[:],
                                 start=True, stop=True).then_inc(mm_pe, 1)

            over_blocks(pe, [(turn(t0, part1, D, agg_v, 0), 0), (times_w, 1)])

            for l in range(LAYERS):
                t0 = first_pass("table", l) * NB

                def times_wcat(n, j, turn_):
                    pe.wait_ge(turned_a, n + (t0 + 1))
                    pe.wait_ge(xa_v, pair_free(n, j) + t0)
                    pe.wait_ge(own_a, pair_free(n, j) + l * NB)
                    nc.tensor.matmul(ps_o[j % 2][:, 0:D], turned[:, j, 0:D],
                                     wcat[:, l, 2 * D:3 * D], start=True, stop=True)
                    nc.tensor.matmul(ps_m[j % 2][:, 0:2 * D], turned[:, j, 0:D],
                                     wcat[:, l, 0:2 * D], start=True, stop=True
                                     ).then_inc(mm_pe, 1)

                over_blocks(pe, [(turn(t0, znorm, D, z_v, 2 * l * NB), 0), (times_wcat, 1)])
                ends(l + 1)

                t0 = first_pass("stats", l) * NB

                def times_wagg(n, j, turn_):
                    pe.wait_ge(turned_a, n + (t0 + 1))
                    pe.wait_ge(x_v, pair_free(n, j) + x_pass("stats", l) * NB)
                    for c in range(4):
                        last = nc.tensor.matmul(ps_m[j % 2][:, 0:3 * D],
                                                turned[:, j, c * D:(c + 1) * D], wagg[:, l, c],
                                                start=(c == 0), stop=(c == 3))
                    last.then_inc(mm_pe, 1)

                over_blocks(pe, [(turn(t0, agg, 4 * D, std_a, l * NB), 0), (times_wagg, 1)])

                t0 = first_pass("mlp", l) * NB

                def times_w1(n, j, turn_):
                    pe.wait_ge(turned_a, n + (t0 + 1))
                    pe.wait_ge(hid_a, pair_free(n, j) + l * NB)
                    for c in range(DM // P):
                        last = nc.tensor.matmul(ps_m[j % 2][:, c * P:(c + 1) * P],
                                                w1[:, l, c * P:(c + 1) * P], turned[:, j, 0:D],
                                                start=True, stop=True)
                    last.then_inc(mm_pe, 1)

                def times_w2(n, j, turn_):
                    pe.wait_ge(hid_a, n + (l * NB + 1))
                    pe.wait_ge(xa_v, pair_free(n, j) + t0)
                    for c in range(DM // P):
                        last = nc.tensor.matmul(ps_o[j % 2][:, 0:D],
                                                hid[:, j, c * P:(c + 1) * P], w2[:, l, c],
                                                start=(c == 0), stop=(c == DM // P - 1))
                    last.then_inc(out_pe, 1)

                over_blocks(pe, [(turn(t0, znorm, D, z_v, (2 * l + 1) * NB), 0), (times_w1, 1),
                                 (times_w2, 2)])

        @block.vector
        def _(dve):
            dve.memset(prev_i[:], -1).then_inc(blank, 1)
            dve.memset(post[:], 0.0)
            dve.memset(wcat[:], 0.0).then_inc(blank, 1)
            dve.memset(zero_b[:], 0.0)
            dve.memset(ones[:], 1.0)
            dve.memset(epsc[:], EPS)
            dve.memset(carry[:], 0.0)
            dve.memset(state[:, R - 1, G - 1], 0.0)
            step = [0]

            def mark(ins):
                step[0] += 1
                ins.then_inc(prep, 1)
                dve.wait_ge(prep, step[0])

            def after(ins):
                return mark(ins)

            dve.wait_ge(iotas, 1)
            nc.vector.tensor_copy(iota_f[:], iota_i[:])
            nc.vector.tensor_copy(iota_b[:], iota_i[:])
            nc.vector.tensor_copy(base_f[:], base_i[:])
            after(nc.vector.tensor_copy(lane_f[:], lane_i[:]))
            nc.vector.tensor_scalar(ident[:], iota_f[:], lane_f[:, 0:1], None, ALU.is_equal)
            nc.vector.tensor_scalar(tri[:], iota_f[:], lane_f[:, 0:1], None, ALU.is_ge
                                    ).then_inc(consts, 1)

            dve.wait_ge(edges_in, 64)
            nc.vector.tensor_copy(dst_f[:], dst_i[:])
            nc.vector.tensor_copy(prev_f[:], prev_i[:])
            nc.vector.tensor_single_scalar(part_i[:, 0], dst_i[:], P - 1, ALU.bitwise_and)
            after(nc.vector.tensor_single_scalar(part_i[:, 1], dst_i[:], P.bit_length() - 1,
                                                 ALU.logical_shift_right))
            after(nc.vector.tensor_copy(part_f[:], part_i[:]))

            with dve.Fori(0, K // HC // 2) as i:
                for h in range(2):
                    if h == 0:
                        dve.wait_ge(counted, i * 2)
                    for k in range(HC):
                        nc.vector.tensor_scalar(
                            onehot_lo[:, h, k], iota_b[:],
                            part_f[:, 0, bass.ds(i * (2 * HC) + (h * HC + k), 1)], None,
                            ALU.is_equal)
                    digits = part_f[:, 1, bass.ds(i * (2 * HC) + h * HC, HC)]
                    nc.vector.tensor_tensor(
                        onehot_hi[:, h], digits.unsqueeze(2).to_broadcast([P, HC, SPREAD]),
                        iota_f[:, 0:SPREAD].unsqueeze(1).to_broadcast([P, HC, SPREAD]),
                        ALU.is_equal).then_inc(coded, 1)

            def norm_stats(source, wait):
                def stats(n, j, turn):
                    dve.wait_ge(x_in, 16)
                    if wait is not None:
                        dve.wait_ge(wait[0], n + (wait[1] + 1))
                    at = (bn[:, 6 * n:6 * n + 6] if isinstance(n, int)
                          else bn[:, bass.ds(n * 6, 6)])
                    nc.vector.bn_stats(at, blk(source, n)).then_inc(bn_v, 1)

                return stats

            def norm_moments(t):
                def own_step(ins):
                    moments[0] += 1
                    ins.then_inc(moment_v, 1)
                    dve.wait_ge(moment_v, moments[0])

                dve.wait_ge(bn_v, NB * (t + 1))
                nc.vector.tensor_tensor(mean[:], bn3[:, :, 1], bn3[:, :, 4], ALU.add)
                nc.vector.tensor_tensor(gap[:], bn3[:, :, 1], bn3[:, :, 4], ALU.subtract)
                own_step(nc.vector.tensor_tensor(vsum[:], bn3[:, :, 2], bn3[:, :, 5], ALU.add))
                nc.vector.tensor_scalar(mean[:], mean[:], 0.5, None, ALU.mult)
                own_step(nc.vector.scalar_tensor_tensor(out=gap[:], in0=gap[:], scalar=0.25,
                                                        in1=gap[:], op0=ALU.mult, op1=ALU.mult))
                nc.vector.scalar_tensor_tensor(out=rowvar[:], in0=vsum[:], scalar=1.0 / D,
                                               in1=gap[:], op0=ALU.mult, op1=ALU.add
                                               ).then_inc(moment_v, 1)
                moments[0] += 1

            moments = [0]

            def norm_scalars(t):
                norm_moments(t)
                dve.wait_ge(root_a, t + 1)
                nc.vector.reciprocal(rstd[:], std_t[:]).then_inc(nrm_v, 1)
                dve.wait_ge(nrm_v, t + 1)
                nc.vector.scalar_tensor_tensor(out=nmr[:], in0=mean[:], scalar=-1.0,
                                               in1=rstd[:], op0=ALU.mult, op1=ALU.mult
                                               ).then_inc(norm_v, 1)

            dve.wait_ge(x_in, 16)
            stats = norm_stats(xin, None)
            over_blocks(dve, [(stats, 0)])
            norm_scalars(norm_pass("lead"))

            after(nc.vector.memset(keep[:, 0:1], 0.0))
            nc.vector.tensor_tensor(keep[:, 1:K], dst_f[:, 1:K], dst_f[:, 0:K - 1], ALU.is_equal)
            nc.vector.tensor_tensor(carry_in[:], dst_f[:, 0:1], prev_f[:], ALU.is_equal)
            nc.vector.tensor_tensor(pass_on[:], dst_f[:, 0:1], dst_f[:, K - 1:K], ALU.is_equal)
            after(nc.vector.tensor_scalar(part_f[:, 0], dst_f[:], dst_f[:, 0:1], 0.0, ALU.is_equal,
                                          ALU.add, accum_out=runlen[:]))
            nc.vector.tensor_scalar(lim[:], keep[:], -0.5, 2 * BIG, ALU.add, ALU.mult)
            nc.vector.tensor_scalar(carry_lim[:], carry_in[:], -0.5, 2 * BIG, ALU.add, ALU.mult)
            nc.vector.scalar_tensor_tensor(out=fix_i[:], in0=runlen[:], scalar=-1.0, in1=base_f[:],
                                           op0=ALU.add, op1=ALU.add)
            after(nc.vector.tensor_tensor(pass_on[:], pass_on[:], carry_in[:], ALU.mult))
            after(nc.vector.tensor_scalar(diag[:], ident[:], pass_on[:, 0:1], None, ALU.mult))

            dve.wait_ge(counted, K // HC + 1)
            nc.vector.tensor_copy(cnt[:], ps_c[:, 0:NB]).then_inc(cnt_ready, 1)
            dve.wait_ge(cnt_ready, 1)
            nc.vector.tensor_scalar(dis[:], cnt[:], 2.0, 1.0, ALU.mult, ALU.max
                                    ).then_inc(dis_in, 1)
            nc.vector.tensor_scalar(has[:], cnt[:], 0.0, None, ALU.is_gt)
            after(nc.vector.tensor_scalar(deg[:], cnt[:], 1.0, None, ALU.max))
            nc.vector.tensor_scalar(amp[:], deg[:], 1.0, None, ALU.add).then_inc(log_in, 1)
            nc.vector.tensor_scalar(nhas[:], has[:], -1.0, None, ALU.mult)
            after(nc.vector.reciprocal(tmpn[:, 2], deg[:]))
            nc.vector.tensor_tensor(inv[:], tmpn[:, 2], has[:], ALU.mult)
            dve.wait_ge(dis_root, 1)
            after(nc.vector.reciprocal(tmpn[:, 3], tmpn[:, 0]))
            nc.vector.tensor_tensor(dis[:], tmpn[:, 3], has[:], ALU.mult).then_inc(dis_ready, 1)
            dve.wait_ge(dis_ready, 1)
            nc.vector.tensor_scalar(dis2[:], dis[:], 2.0, None, ALU.mult)
            dve.wait_ge(prefix_t, 1)
            nc.vector.tensor_copy(pass_row[:], ps_s[:, P:2 * P])
            nc.vector.tensor_scalar(pass_lim[:], ps_s[:, P:2 * P], -0.5, 2 * BIG, ALU.add, ALU.mult)
            after(nc.vector.tensor_copy(tot[:], ps_s[:, SPREAD:SPREAD + NB]))
            after(nc.vector.tensor_tensor_scan(totscan[:], ones[:, 0:NB], tot[:], 0.0,
                                               ALU.mult, ALU.add))
            after(nc.vector.tensor_tensor(tot[:], totscan[:], tot[:], ALU.subtract))
            after(nc.vector.tensor_tensor(end_f[:], ps_s[:, 0:NB], tot[:], ALU.add))
            after(nc.vector.tensor_scalar(end_i[:], end_f[:], -1.0, 0.0, ALU.add, ALU.max))
            dve.wait_ge(logs, 1)
            nc.vector.tensor_scalar(amp[:], tmpn[:, 1], 1.0 / AVG_LOG, None, ALU.mult)
            after(nc.vector.reciprocal(tmpn[:, 4], tmpn[:, 1]))
            nc.vector.tensor_scalar(att[:], tmpn[:, 4], AVG_LOG, None, ALU.mult)
            for g in range(R):
                nc.vector.tensor_copy(idx[:, g], src_i[:, g * G:(g + 1) * G]
                                      ).then_inc(idx_ready[g], 1)

            def scan_phase(q):
                before = scanned_before(q)
                per = per_step(q)
                with dve.Fori(0, ITERS) as i:
                    for g in range(R):
                        if q == 0:
                            dve.wait_ge(gathered[g], i * (16 * G) + 16 * G)
                        else:
                            dve.wait_ge(lifted, i * R + ((q - 1) * GROUPS + g + 1))
                        dve.wait_ge(stored[g], i * 16 + 16 * ITERS * q)
                        for j in range(G):
                            k = i * (R * G) + (g * G + j)
                            pg, pj = (g, j - 1) if j else ((g - 1) % R, G - 1)
                            done = i * (R * G * per) + (before + (g * G + j) * per)
                            if q > 0:
                                dve.wait_ge(scanned, done - 1)
                                nc.vector.scalar_tensor_tensor(
                                    out=state[:, g, j, 0:2 * D], in0=state[:, pg, pj, 0:2 * D],
                                    scalar=lim[:, bass.ds(k, 1)], in1=rows[:, g, j, 0:2 * D],
                                    op0=ALU.min, op1=ALU.max).then_inc(scanned, 1)
                            lo, hi = (2 * D, 3 * D) if q == 0 else (2 * D, 4 * D)
                            dve.wait_ge(scanned, done)
                            nc.vector.scalar_tensor_tensor(
                                out=state[:, g, j, lo:hi], in0=state[:, pg, pj, lo:hi],
                                scalar=keep[:, bass.ds(k, 1)], in1=rows[:, g, j, D:hi - D],
                                op0=ALU.mult, op1=ALU.add).then_inc(scanned, 1)
                        dve.wait_ge(scanned, i * (R * G * per) + (before + (g + 1) * G * per))
                        nc.vector.tensor_copy(
                            idx[:, g], src_i[:, bass.ds(i * (R * G) + (R + g) * G, G)]
                        ).then_inc(idx_ready[g], 1)
                dve.wait_ge(ends_t, q + 1)
                scans = [(pass_row, ALU.mult, ALU.add)] if q == 0 else (
                    [(pass_lim, ALU.min, ALU.max)] * 2 + [(pass_row, ALU.mult, ALU.add)] * 2)
                for a, (mask, op0, op1) in enumerate(scans):
                    last = nc.vector.tensor_tensor_scan(carry[:, a, 1:P + 1], mask[:],
                                                        ps_c[:, a * P:(a + 1) * P], 0.0, op0, op1)
                last.then_inc(carried, 1)
                dve.wait_ge(carry_t, q + 1)
                dve.wait_ge(fix_in, 16 * (q + 1))
                if q == 0:
                    nc.vector.scalar_tensor_tensor(
                        out=fixed[:, 0:D], in0=ps_s[:, 0:D], scalar=carry_in[:, 0:1],
                        in1=fixrow[:, 0:D], op0=ALU.mult, op1=ALU.add).then_inc(fix_v, 1)
                else:
                    nc.vector.scalar_tensor_tensor(
                        out=fixed[:, 0:2 * D], in0=ps_s[:, 0:2 * D], scalar=carry_lim[:, 0:1],
                        in1=fixrow[:, 0:2 * D], op0=ALU.min, op1=ALU.max).then_inc(fix_v, 1)
                    nc.vector.scalar_tensor_tensor(
                        out=fixed[:, 2 * D:4 * D], in0=ps_s[:, 2 * D:4 * D],
                        scalar=carry_in[:, 0:1], in1=fixrow[:, 2 * D:4 * D],
                        op0=ALU.mult, op1=ALU.add).then_inc(fix_v, 1)

            dve.wait_ge(small_in, n_small)
            for l in range(LAYERS):
                nc.vector.tensor_scalar(postbc[:, l], ones[:], bpostc[:, l:l + 1], None, ALU.mult
                                        ).then_inc(post_bc, 1)

            scan_phase(0)
            for l in range(LAYERS):
                dve.wait_ge(post_row, l + 1)
                nc.vector.tensor_tensor(hrow[:, l], ps_m[0][:, l * D:(l + 1) * D], blinrow[:, l], ALU.add
                                        ).then_inc(hrow_v, 1)

            t0 = first_pass("first") * NB

            def first_rows(n, j, turn):
                dve.wait_ge(nst_in[j], turn * 16 + 16)
                dve.wait_ge(turned_pe, ring_free(n) + t0)
                nc.vector.scalar_tensor_tensor(
                    out=part1[:, j], in0=nst[:, j, 0:D], scalar=col(dis2, n), in1=blk(acc, n),
                    op0=ALU.mult, op1=ALU.add).then_inc(agg_v, 1)

            def first_bias(n, j, turn):
                dve.wait_ge(mm_pe, n + (t0 + 1))
                nc.vector.tensor_tensor(part2[:, j], ps_m[j % 2][:, 0:D], b0row[:], ALU.add
                                        ).then_inc(xa_v, 1)

            def first_x(n, j, turn):
                dve.wait_ge(xa_v, n + (t0 + 1))
                nc.vector.scalar_tensor_tensor(
                    out=blk(xin, n), in0=part2[:, j], scalar=0.0, in1=blk(xin, n), op0=ALU.max,
                    op1=ALU.add).then_inc(x_v, 1)

            stats = norm_stats(xin, (x_v, x_pass("first") * NB))
            over_blocks(dve, [(first_rows, 0), (first_bias, 2), (first_x, 3), (stats, 4)])
            norm_scalars(norm_pass("first"))
            stats = norm_stats(cur, (relu_a, NB))
            over_blocks(dve, [(stats, 0)])
            norm_scalars(norm_pass("relu"))

            for l in range(LAYERS):
                def normalise(t, zbase):
                    def stage(n, j, turn):
                        dve.wait_ge(norm_v, norm_of[0] + 1)
                        dve.wait_ge(turned_pe, ring_free(n) + t)
                        nc.vector.tensor_scalar(znorm[:, j], blk(cur, n), col(rstd, n),
                                                col(nmr, n), ALU.mult, ALU.add).then_inc(z_v, 1)
                    return stage

                t0 = first_pass("table", l) * NB
                norm_of = [norm_pass("relu") if l == 0 else norm_pass("mlp", l - 1)]

                def take_b(n, j, turn):
                    dve.wait_ge(mm_pe, n + (t0 + 1))
                    dve.wait_ge(bout_st[j], turn * 16 + 16 * (NB // U) * l)
                    nc.vector.tensor_tensor(bout[:, j], ps_m[j % 2][:, 0:D], bprerow[:, l],
                                            ALU.add).then_inc(bout_v, 1)
                    nc.vector.tensor_tensor(part1[:, j], ps_m[j % 2][:, D:2 * D], blk(cur, n),
                                            ALU.add).then_inc(xa_v, 1)

                def take_acc(n, j, turn):
                    dve.wait_ge(xa_v, n + (t0 + 1))
                    nc.vector.tensor_tensor(blk(acc, n), part1[:, j], hrow[:, l], ALU.add
                                            ).then_inc(acc_v, 1)

                over_blocks(dve, [(normalise(t0, 2 * l * NB), 0), (take_b, 2), (take_acc, 3)])
                scan_phase(l + 1)

                t0 = first_pass("stats", l) * NB

                def aggregates(n, j, turn):
                    dve.wait_ge(nst_in[j], turn * 16 + 16 * (NB // U * (l + 1) + 1))
                    dve.wait_ge(turned_pe, ring_free(n) + t0)
                    for at, st, scalar in ((0, 2, inv), (1, 0, nhas), (2, 1, has)):
                        nc.vector.scalar_tensor_tensor(
                            out=agg[:, j, at * D:(at + 1) * D], in0=nst[:, j, st * D:(st + 1) * D],
                            scalar=col(scalar, n), in1=blk(own, n), op0=ALU.mult, op1=ALU.add)
                    dve.wait_ge(sq_a, n + (l * NB + 1))
                    nc.vector.scalar_tensor_tensor(
                        out=var[:, j], in0=nst[:, j, 3 * D:4 * D], scalar=col(inv, n),
                        in1=msq[:, j], op0=ALU.mult, op1=ALU.subtract).then_inc(var_v, 1)

                def clamp_var(n, j, turn):
                    dve.wait_ge(var_v, n + (l * NB + 1))
                    nc.vector.tensor_scalar(var[:, j], var[:, j], 0.0, None, ALU.max
                                            ).then_inc(agg_v, 1)

                def add_amp(n, j, turn):
                    dve.wait_ge(mm_pe, n + (t0 + 1))
                    nc.vector.scalar_tensor_tensor(
                        out=part1[:, j], in0=ps_m[j % 2][:, D:2 * D], scalar=col(amp, n),
                        in1=blk(acc, n), op0=ALU.mult, op1=ALU.add).then_inc(xa_v, 1)
                    dve.wait_ge(xa_v, n + (t0 + 1))
                    nc.vector.scalar_tensor_tensor(
                        out=part2[:, j], in0=ps_m[j % 2][:, 2 * D:3 * D], scalar=col(att, n),
                        in1=part1[:, j], op0=ALU.mult, op1=ALU.add).then_inc(xb_v, 1)
                    dve.wait_ge(xb_v, n + (l * NB + 1))
                    nc.vector.tensor_tensor(blk(cur, n), ps_m[j % 2][:, 0:D], part2[:, j], ALU.add
                                            ).then_inc(x_v, 1)

                stats = norm_stats(cur, (x_v, x_pass("stats", l) * NB))
                over_blocks(dve, [(aggregates, 0), (clamp_var, 1), (add_amp, 3), (stats, 4)])
                norm_scalars(norm_pass("stats", l))

                t0 = first_pass("mlp", l) * NB
                norm_of = [norm_pass("stats", l)]

                def add_bias(n, j, turn):
                    dve.wait_ge(out_pe, n + (l * NB + 1))
                    nc.vector.tensor_tensor(part1[:, j], ps_o[j % 2][:, 0:D], b2row[:, l], ALU.add
                                            ).then_inc(xa_v, 1)

                def add_mlp(n, j, turn):
                    dve.wait_ge(xa_v, n + (t0 + 1))
                    nc.vector.tensor_tensor(blk(cur, n), part1[:, j], blk(cur, n), ALU.add
                                            ).then_inc(x_v, 1)

                def add_outer(n, j, turn):
                    dve.wait_ge(x_v, n + (x_pass("mlp", l) * NB + 1))
                    nc.vector.tensor_tensor(blk(acc, n), blk(cur, n), blk(xin, n), ALU.add
                                            ).then_inc(out_v, 1)

                if l < LAYERS - 1:
                    stats = norm_stats(cur, (x_v, x_pass("mlp", l) * NB))
                    tail = [(stats, 5)]
                else:
                    tail = [(add_outer, 5)]
                over_blocks(dve, [(normalise(t0, 0), 0), (add_bias, 3), (add_mlp, 4)] + tail)
                if l < LAYERS - 1:
                    norm_scalars(norm_pass("mlp", l))


def kernel(x, src, dst, **p):
    import concourse.bacc as bacc
    from concourse.bass_utils import run_bass_kernel_spmd

    arrays = {
        "x": np.pad(np.asarray(x), ((0, NB * P - N), (0, 0))),
        "src": np.pad(np.asarray(src), (0, P * K - E)),
        "dst": np.pad(np.asarray(dst), (0, P * K - E), constant_values=P * SPREAD - 1),
    }
    names = ["L0_gnn_W", "L0_gnn_b"] + ["L1_gnn_" + k for k in (
        "ln1_g", "ln1_b", "W_pre", "b_pre", "W_post", "b_post", "W_lin", "b_lin", "ln2_g", "ln2_b",
        "W1", "b1", "W2", "b2")]
    for name in names:
        arrays[name] = np.ascontiguousarray(p[name])
    nc = bacc.Bacc("TRN2", target_bir_lowering=False, num_devices=1)
    args = [nc.dram_tensor(f"in_{k}", a.shape, mybir.dt.from_np(a.dtype), kind="ExternalInput").ap()
            for k, a in arrays.items()]
    out = nc.dram_tensor("out", (NB * P, D), F32, kind="ExternalOutput").ap()
    graph_layers(nc, *args, out)
    r = run_bass_kernel_spmd(nc, [{f"in_{k}": a for k, a in arrays.items()}], core_ids=[0])
    return r.results[0]["out"][:N]
```
